# Optimizing a Trainium2 kernel written in Bass

```python
import numpy as np
import jax
import jax.numpy as jnp

def _softmax(x, axis=-1):
    return jax.nn.softmax(x, axis=axis)

def _gelu(x):
    return jax.nn.gelu(x, approximate=True)

def _silu(x):
    return jax.nn.silu(x)

def _sigmoid(x):
    return jax.nn.sigmoid(x)

def _layernorm(x, axis=-1, eps=1e-05):
    m = jnp.mean(x, axis=axis, keepdims=True)
    v = jnp.var(x, axis=axis, keepdims=True)
    return (x - m) / jnp.sqrt(v + eps)

def _scatter_add(tgt, idx, src, axis=0):
    return tgt.at[idx].add(src)

def _segment_sum(src, seg, n):
    return jax.ops.segment_sum(src, seg, n)
kernel_name = 'mk_rec_standalone_d1_rec_r8_19b5a3'

def setup_inputs(seed: int=0):
    np.random.seed(seed)
    _w = jnp.asarray

    def _rec_inputs():
        import jax
        import jax.numpy as jnp
        _rk = jax.random.key(seed)
        r_x = 7.22013e-05 + 1.00017 * jax.random.normal(jax.random.fold_in(_rk, 1), (2048, 32, 64), jnp.float32)
        return r_x
    r_x = _rec_inputs()

    def _L0_rec_setup():
        import jax, jax.numpy as jnp
        import numpy as np
        from itertools import combinations
        NUM_FIELDS = 32
        INPUT_DIM = 64
        BATCH = 512
        PAIRS = np.array(list(combinations(range(NUM_FIELDS), 2)), dtype=np.int32)
        key = jax.random.key(seed)
        k1, k2 = jax.random.split(key)
        x = jax.random.normal(k1, (BATCH, NUM_FIELDS, INPUT_DIM), dtype=jnp.float32)
        W = jax.random.normal(k2, (PAIRS.shape[0], INPUT_DIM, INPUT_DIM), dtype=jnp.float32) * 0.05
        return {'x': x, 'W': W}
    _L0_rec_all = _L0_rec_setup()
    _L0_rec_in = {k: v for k, v in _L0_rec_all.items() if k in ('W',)}
    del _L0_rec_all
    return {'r_x': r_x, 'L0_rec_W': _L0_rec_in['W']}

def reference(r_x, L0_rec_W):
    import jax
    import jax.numpy as jnp

    def _L0_rec_ref(x, W):
        import jax, jax.numpy as jnp
        import numpy as np
        from itertools import combinations
        NUM_FIELDS = 32
        INPUT_DIM = 64
        BATCH = 512
        PAIRS = np.array(list(combinations(range(NUM_FIELDS), 2)), dtype=np.int32)
        pi = jnp.asarray(PAIRS[:, 0])
        pj = jnp.asarray(PAIRS[:, 1])
        xi = x[:, pi, :]
        xj = x[:, pj, :]
        proj = jnp.einsum('bpd,pod->bpo', xi, W)
        return proj * xj
    y = _L0_rec_ref(r_x, L0_rec_W)
    return y

_drawn_inputs = setup_inputs


def setup_inputs(seed=0):
    import zlib

    import numpy as np

    out = dict(_drawn_inputs(seed))
    spreads = {}
    factors = {}
    for name, (base, spread) in spreads.items():
        noise = np.random.default_rng([zlib.crc32(name.encode()), seed]).standard_normal(out[name].shape)
        drawn = base * np.exp(spread * noise) if base else spread * noise
        out[name] = jnp.asarray(drawn.astype(out[name].dtype))
    for name, factor in factors.items():
        out[name] = (out[name] * factor).astype(out[name].dtype)
    return out
```

```python
from contextlib import ExitStack

import concourse.bass as bass
from concourse import mybir

F32 = mybir.dt.float32
F32R = mybir.dt.float32r
I32 = mybir.dt.int32
ALU = mybir.AluOpType
ACT = mybir.ActivationFunctionType

P = 128
BANK = 512
HI_BITS = -4096
PROJ_BUFS = 3
SLOTS = 5
CHUNK = 4
W_CHUNK = 16
W_RING = 4
W_LEAD_PE = 1
W_LEAD_DVE = W_LEAD_PE + 2


def pair_index(i, j, fields):
    return i * (2 * fields - i - 1) // 2 + (j - i - 1)


def plan(fields, dim):
    fit = 2 * BANK // dim
    def whole(*lengths):
        return [(fields - 1 - n, fields - n, n) for n in lengths]
    groups = []
    for i in range(fields - 1 - fit):
        n = fields - 1 - i
        groups.append([[(i, i + 1, n - n // 2)], [(i, i + 1 + n - n // 2, n // 2)]])
    groups += [[whole(16), whole(15)], [whole(14), whole(13)], [whole(12), whole(11)],
               [whole(10), whole(9), whole(8)], [whole(7, 6), whole(5, 4), whole(3, 2, 1)]]
    return groups


class Tile:
    def __init__(self, number, parity, half, last=False):
        self.number, self.parity, self.half, self.last = number, parity, half, last
        self.first = isinstance(number, int) and number == 0

    def next(self):
        return Tile(self.number + 1, 1 - self.parity, self.half + self.parity)


def field_pair_project(nc, x, w, ident, out, fields, dim):
    batch = x.shape[0]
    tiles = batch // P
    groups = plan(fields, dim)
    steps = [step for group in groups for step in group]
    n_steps, n_groups, chunks = len(steps), len(groups), fields // CHUNK
    pairs = fields * (fields - 1) // 2
    w_chunks = pairs // W_CHUNK
    uses = n_steps // PROJ_BUFS
    slot_uses = n_groups // SLOTS
    assert n_steps % PROJ_BUFS == 0 and n_groups % SLOTS == 0 and chunks % 2 == 0
    assert tiles % 2 == 0 and tiles >= 4 and pairs % W_CHUNK == 0 and 2 * dim == P

    def group_range(group):
        i, j0, _ = group[0][0]
        k, l0, n = group[-1][-1]
        return pair_index(i, j0, fields), pair_index(k, l0 + n - 1, fields) + 1
    slot_pairs = max(end - first for first, end in map(group_range, groups))

    chunk_starts = {min(s for s, step in enumerate(steps) if step[0][0] >= CHUNK * c): c for c in range(chunks)}
    w_needed = [pair_index(step[-1][0], step[-1][1] + step[-1][2] - 1, fields) // W_CHUNK for step in steps]

    def w_due(s, lead):
        before = min(w_needed[s - 1] + lead, w_chunks - 1) if s else -1
        return range(before + 1, min(w_needed[s] + lead, w_chunks - 1) + 1)

    def transposes_due(tile, s):
        due = []
        if tile.first:
            if s == 0:
                due.append(("x", tile, 0))
            due += [("w", k) for k in w_due(s, W_LEAD_PE)]
        if s in chunk_starts:
            c = chunk_starts[s] + 1
            if c < chunks:
                due.append(("x", tile, c))
            elif not tile.last:
                due.append(("x", tile.next(), 0))
        return due

    def each_tile(eng, emit):
        emit(Tile(0, 0, 0))
        with eng.Fori(0, (tiles - 2) // 2) as t:
            emit(Tile(2 * t + 1, 1, t))
            emit(Tile(2 * t + 2, 0, t + 1))
        emit(Tile(tiles - 1, 1, tiles // 2 - 1, last=True))

    with ExitStack() as ctx:
        def sb(name, shape, dt=F32):
            return ctx.enter_context(nc.sbuf_tensor(name, shape, dt))

        def psum(name, cols):
            return ctx.enter_context(nc.psum_tensor(name, [P, cols], F32))

        def sem(name):
            return ctx.enter_context(nc.semaphore(name))

        w_t = sb("w_t", [P, pairs * dim], F32R)
        x_sb = [sb(f"x_sb{h}", [P, fields * dim]) for h in range(2)]
        x_parts = [sb(f"x_parts{h}", [P, CHUNK, 3, dim]) for h in range(2)]
        x_t = [sb(f"x_t{h}", [P, CHUNK, 2, P], F32R) for h in range(2)]
        w_parts = [sb(f"w_parts{h}", [P, W_CHUNK // 2, 2, dim]) for h in range(2)]
        w_in = [x_sb[1][:, r * W_CHUNK // 2 * dim:(r + 1) * W_CHUNK // 2 * dim] for r in range(W_RING)]
        ident_sb = sb("ident_sb", [P, P])
        staged = [sb(f"staged{s}", [P, slot_pairs * dim]) for s in range(SLOTS)]
        proj = [psum(f"proj{b}", 2 * BANK) for b in range(PROJ_BUFS)]
        turned = [psum(f"turned{k}", BANK) for k in range(2)]

        ident_loaded = sem("ident_loaded")
        x_loaded = [sem(f"x_loaded{h}") for h in range(2)]
        w_loaded = [sem(f"w_loaded{r}") for r in range(W_RING)]
        x_hi_done = sem("x_hi_done")
        x_parts_done = sem("x_parts_done")
        x_turned = [sem(f"x_turned{k}") for k in range(2)]
        x_t_done = [sem(f"x_t_done{k}") for k in range(2)]
        w_hi_done = sem("w_hi_done")
        w_lo_done = sem("w_lo_done")
        w_turned = [sem(f"w_turned{k}") for k in range(2)]
        w_t_done = [sem(f"w_t_done{k}") for k in range(2)]
        projected = [sem(f"projected{b}") for b in range(PROJ_BUFS)]
        scaled = [sem(f"scaled{b}") for b in range(PROJ_BUFS)]
        stored = [sem(f"stored{s}") for s in range(SLOTS)]

        block = ctx.enter_context(nc.Block())

        @block.sync
        def _(sp):
            def load_w(k):
                if k >= W_RING:
                    sp.wait_ge(w_lo_done, k - W_RING + 1)
                at = k * W_CHUNK // 2 * dim
                sp.dma_start(w_in[k % W_RING], w[:, at:at + W_CHUNK // 2 * dim]).then_inc(w_loaded[k % W_RING], 16)

            def emit(tile):
                s = -1
                for g, group in enumerate(groups):
                    if tile.first:
                        ahead = w_needed[min(s + len(group) + 2, n_steps - 1)] + W_LEAD_DVE + 1
                        while w_next[0] < min(ahead, w_chunks):
                            load_w(w_next[0])
                            w_next[0] += 1
                            if w_next[0] == w_chunks:
                                sp.wait_ge(w_lo_done, w_chunks)
                                sp.dma_start(x_sb[1][:], x[P:2 * P, :]).then_inc(x_loaded[1], 16)
                    first, end = group_range(group)
                    s += len(group)
                    sp.wait_ge(scaled[s % PROJ_BUFS], tile.number * uses + s // PROJ_BUFS + 1)
                    sp.dma_start(out[bass.ds(tile.number * P, P), first * dim:end * dim],
                                 staged[g % SLOTS][:, 0:(end - first) * dim]).then_inc(stored[g % SLOTS], 16)

            def load_x(tile):
                sp.wait_ge(x_parts_done, (tile.number + 1) * 2 * chunks)
                sp.dma_start(x_sb[tile.parity][:], x[bass.ds((tile.number + 2) * P, P), :]
                             ).then_inc(x_loaded[tile.parity], 16)

            w_next = [W_RING]
            load_w(0)
            sp.dma_start(x_sb[0][:], x[0:P, :]).then_inc(x_loaded[0], 16)
            for k in range(1, W_RING):
                load_w(k)
            tile = Tile(0, 0, 0)
            emit(tile)
            load_x(tile)
            with sp.Fori(0, (tiles - 4) // 2) as t:
                for tile in (Tile(2 * t + 1, 1, t), Tile(2 * t + 2, 0, t + 1)):
                    emit(tile)
                    load_x(tile)
            tile = Tile(tiles - 3, 1, tiles // 2 - 2)
            emit(tile)
            load_x(tile)
            emit(Tile(tiles - 2, 0, tiles // 2 - 1))
            emit(Tile(tiles - 1, 1, tiles // 2 - 1, last=True))
            for slot in range(SLOTS):
                sp.wait_ge(stored[slot], 16 * slot_uses * tiles)

        @block.gpsimd
        def _(pool):
            def split_x(tile, c):
                parts = x_parts[c % 2]
                cols = slice(c * CHUNK * dim, (c + 1) * CHUNK * dim)
                pool.wait_ge(x_hi_done, tile.number * chunks + c + 1)
                nc.gpsimd.tensor_tensor(parts[:, :, 1, :], x_sb[tile.parity][:, cols].rearrange(
                    "p (f d) -> p f d", d=dim), parts[:, :, 0, :], ALU.subtract).then_inc(x_parts_done, 1)
                nc.gpsimd.tensor_copy(parts[:, :, 2, :], parts[:, :, 0, :]).then_inc(x_parts_done, 1)

            def split_w(k):
                pool.wait_ge(w_hi_done, k + 1)
                parts = w_parts[k % 2]
                nc.gpsimd.tensor_tensor(parts[:, :, 1, :], w_in[k % W_RING].rearrange("p (q d) -> p q d", d=dim),
                                        parts[:, :, 0, :], ALU.subtract).then_inc(w_lo_done, 1)

            def emit(tile):
                for s in range(n_steps):
                    if tile.first:
                        if s == 0:
                            split_x(tile, 0)
                        for k in w_due(s, W_LEAD_DVE):
                            split_w(k)
                            if k == 0:
                                split_x(tile, 1)
                    if s in chunk_starts:
                        c = chunk_starts[s] + 2
                        if c < chunks:
                            split_x(tile, c)
                        elif not tile.last:
                            split_x(tile.next(), c - chunks)

            each_tile(pool, emit)

        @block.scalar
        def _(act):
            act.dma_start(ident_sb[:], ident).then_inc(ident_loaded, 16)

            def emit(tile):
                for s in range(n_steps):
                    for what in transposes_due(tile, s):
                        for k in range(2):
                            if what[0] == "x":
                                _, of, c = what
                                act.wait_ge(x_turned[k], of.number * chunks + c + 1)
                                nc.scalar.activation(x_t[c % 2][:, 2 * k:2 * k + 2, :, :].rearrange(
                                    "p f v b -> p (f v b)"), turned[k][:], ACT.Copy).then_inc(x_t_done[k], 1)
                            else:
                                chunk = what[1]
                                act.wait_ge(w_turned[k], chunk + 1)
                                at = chunk * W_CHUNK * dim + k * BANK
                                nc.scalar.activation(w_t[:, at:at + BANK], turned[k][:],
                                                     ACT.Copy).then_inc(w_t_done[k], 1)

            each_tile(act, emit)

        @block.tensor
        def _(pe):
            turned_before = [None]

            def transpose(what):
                before = turned_before[0]
                turned_before[0] = what
                if what[0] == "x":
                    _, of, c = what
                    pe.wait_ge(x_parts_done, (of.number * chunks + c + 1) * 2)
                else:
                    pe.wait_ge(w_lo_done, what[1] + 1)
                for k in range(2):
                    if before is not None and before[0] == "w":
                        pe.wait_ge(w_t_done[k], before[1] + 1)
                    elif before is not None:
                        pe.wait_ge(x_t_done[k], before[1].number * chunks + before[2] + 1)
                    for n in range(BANK // P):
                        if what[0] == "x":
                            part = n % 2
                            parts = x_parts[c % 2][:, 2 * k + n // 2, part:part + 2, :]
                        else:
                            parts = w_parts[what[1] % 2][:, k * (BANK // P) + n, :, :]
                        last = nc.tensor.transpose(turned[k][:, n * P:(n + 1) * P],
                                                   parts.rearrange("p v d -> p (v d)"), ident_sb[:])
                    last.then_inc(x_turned[k] if what[0] == "x" else w_turned[k], 1)

            def project(tile, s):
                buf = s % PROJ_BUFS
                if not (tile.first and s < PROJ_BUFS):
                    pe.wait_ge(scaled[buf], tile.number * uses + s // PROJ_BUFS)
                at = 0
                for i, j0, n in steps[s]:
                    col = pair_index(i, j0, fields) * dim
                    left = n * dim
                    while left:
                        width = min(left, BANK - at % BANK)
                        for part in range(2):
                            last = nc.tensor.matmul(
                                proj[buf][:, at:at + width], x_t[i // CHUNK % 2][:, i % CHUNK, part, :],
                                w_t[:, col:col + width], start=part == 0, stop=part == 1)
                        at, col, left = at + width, col + width, left - width
                last.then_inc(projected[buf], 1)

            def emit(tile):
                if not tile.first:
                    turned_before[0] = ("x", tile, 0)
                for s in range(n_steps):
                    for what in transposes_due(tile, s):
                        transpose(what)
                    if s in chunk_starts:
                        for k in range(2):
                            pe.wait_ge(x_t_done[k], tile.number * chunks + chunk_starts[s] + 1)
                    if tile.first:
                        for k in range(2):
                            pe.wait_ge(w_t_done[k], w_needed[s] + 1)
                    project(tile, s)

            pe.wait_ge(ident_loaded, 16)
            each_tile(pe, emit)

        @block.vector
        def _(dve):
            def split_x(tile, c):
                if c == 0:
                    dve.wait_ge(x_loaded[tile.parity], 16 * tile.half + 16)
                if not (tile.first and c < 2):
                    dve.wait_ge(x_turned[1], tile.number * chunks + c - 1)
                cols = slice(c * CHUNK * dim, (c + 1) * CHUNK * dim)
                nc.vector.tensor_scalar(
                    x_parts[c % 2][:, :, 0, :].bitcast(I32),
                    x_sb[tile.parity][:, cols].rearrange("p (f d) -> p f d", d=dim).bitcast(I32),
                    HI_BITS, None, ALU.bitwise_and).then_inc(x_hi_done, 1)

            def split_w(k):
                dve.wait_ge(w_loaded[k % W_RING], 16 * (k // W_RING) + 16)
                if k >= 2:
                    dve.wait_ge(w_turned[1], k - 1)
                nc.vector.tensor_scalar(
                    w_parts[k % 2][:, :, 0, :].bitcast(I32),
                    w_in[k % W_RING].rearrange("p (q d) -> p q d", d=dim).bitcast(I32),
                    HI_BITS, None, ALU.bitwise_and).then_inc(w_hi_done, 1)

            def emit(tile):
                s = 0
                for g, group in enumerate(groups):
                    slot = g % SLOTS
                    start = group_range(group)[0]
                    if not (tile.first and g < SLOTS):
                        dve.wait_ge(stored[slot], tile.number * 16 * slot_uses + 16 * (g // SLOTS))
                    for step in group:
                        if tile.first:
                            if s == 0:
                                split_x(tile, 0)
                            for k in w_due(s, W_LEAD_DVE):
                                split_w(k)
                                if k == 0:
                                    split_x(tile, 1)
                        if s in chunk_starts:
                            c = chunk_starts[s] + 2
                            if c < chunks:
                                split_x(tile, c)
                            elif not tile.last:
                                split_x(tile.next(), c - chunks)
                        buf = s % PROJ_BUFS
                        dve.wait_ge(projected[buf], tile.number * uses + s // PROJ_BUFS + 1)
                        at = 0
                        for i, j0, n in step:
                            to = (pair_index(i, j0, fields) - start) * dim
                            last = nc.vector.tensor_tensor(
                                staged[slot][:, to:to + n * dim], proj[buf][:, at:at + n * dim],
                                x_sb[tile.parity][:, j0 * dim:(j0 + n) * dim], ALU.mult)
                            at += n * dim
                        last.then_inc(scaled[buf], 1)
                        s += 1

            each_tile(dve, emit)


def kernel(r_x, L0_rec_W):
    import numpy as np
    import concourse.bacc as bacc
    from concourse.bass_utils import run_bass_kernel_spmd

    batch, fields, dim = r_x.shape
    pairs = L0_rec_W.shape[0]
    w = np.ascontiguousarray(np.asarray(L0_rec_W).reshape(pairs // 2, 2 * dim, dim).transpose(1, 0, 2))
    arrays = {
        "x_dram": np.ascontiguousarray(r_x).reshape(batch, fields * dim),
        "w_dram": w.reshape(2 * dim, pairs // 2 * dim),
        "ident_dram": np.eye(P, dtype=np.float32),
    }
    nc = bacc.Bacc("TRN2", target_bir_lowering=False, num_devices=1)
    aps = [nc.dram_tensor(n, a.shape, F32, kind="ExternalInput").ap() for n, a in arrays.items()]
    out = nc.dram_tensor("out_dram", (batch, pairs * dim), F32, kind="ExternalOutput").ap()
    field_pair_project(nc, *aps, out, fields, dim)
    r = run_bass_kernel_spmd(nc, [arrays], core_ids=[0])
    return r.results[0]["out_dram"].reshape(batch, pairs, dim)
```

```python
from contextlib import ExitStack

import concourse.bass as bass
from concourse import mybir

F32 = mybir.dt.float32
F32R = mybir.dt.float32r
I32 = mybir.dt.int32
ALU = mybir.AluOpType
ACT = mybir.ActivationFunctionType

P = 128
BANK = 512
HI_BITS = -4096
PROJ_BUFS = 3
SLOTS = 5
CHUNK = 4
POOL_FIELDS = (2, 5, 8, 11, 14)
WARM_UP = 16
W_CHUNK = 16
W_RING = 7
W_SPLIT_SLOTS = (2, 3, 4)
W_LEAD = 1
W_LEAD_FROM = 2
W_GAIN = 4


def pair_index(i, j, fields):
    return i * (2 * fields - i - 1) // 2 + (j - i - 1)


def plan(fields, dim):
    fit = 2 * BANK // dim
    def whole(*lengths):
        return [(fields - 1 - n, fields - n, n) for n in lengths]
    groups = []
    for i in range(fields - 1 - fit):
        n = fields - 1 - i
        cut = fit if n > fit + fit // 2 else fit // 2
        groups.append([[(i, i + 1, cut)], [(i, i + 1 + cut, n - cut)]])
    groups += [[whole(16), whole(15)], [whole(14), whole(13)], [whole(12), whole(11)],
               [whole(10), whole(9), whole(8)], [whole(7, 6), whole(5, 4), whole(3, 2, 1)]]
    return groups


def place(step, dim):
    at, places = 0, []
    for _, _, n in step:
        if at % BANK + n * dim > BANK and n * dim <= BANK:
            at = -(-at // BANK) * BANK
        places.append(at)
        at += n * dim
    assert at <= 2 * BANK
    return places


class Tile:
    def __init__(self, number, parity, half, last=False):
        self.number, self.parity, self.half, self.last = number, parity, half, last
        self.first = isinstance(number, int) and number == 0

    def next(self):
        return Tile(self.number + 1, 1 - self.parity, self.half + self.parity)


def field_pair_project(nc, x, w, ident, out, fields, dim):
    batch = x.shape[0]
    tiles = batch // P
    groups = plan(fields, dim)
    steps = [step for group in groups for step in group]
    n_steps, n_groups, chunks = len(steps), len(groups), fields // CHUNK
    pairs = fields * (fields - 1) // 2
    w_chunks = pairs // W_CHUNK
    uses = n_steps // PROJ_BUFS
    slot_uses = n_groups // SLOTS
    assert n_steps % PROJ_BUFS == 0 and n_groups % SLOTS == 0 and chunks % 2 == 0
    assert tiles % 2 == 0 and tiles >= 4 and pairs % W_CHUNK == 0 and 2 * dim == P

    def group_range(group):
        i, j0, _ = group[0][0]
        k, l0, n = group[-1][-1]
        return pair_index(i, j0, fields), pair_index(k, l0 + n - 1, fields) + 1
    slot_pairs = max(end - first for first, end in map(group_range, groups))

    w_cols = W_CHUNK // 2 * dim
    w_per_slot = slot_pairs * dim // w_cols

    pool_steps = [2 * i + 1 for i in POOL_FIELDS]
    assert all(len(steps[s]) == 1 and steps[s][0][0] == i for s, i in zip(pool_steps, POOL_FIELDS))

    chunk_starts = {min(s for s, step in enumerate(steps) if step[0][0] >= CHUNK * c): c for c in range(chunks)}
    w_needed = [pair_index(step[-1][0], step[-1][1] + step[-1][2] - 1, fields) // W_CHUNK for step in steps]

    def w_turned_by(s):
        if s < 0:
            return 0
        lead = W_LEAD if s >= W_LEAD_FROM else 0
        return min(w_needed[s] + w_needed[s] // W_GAIN + lead + 1, w_chunks)

    def w_split_by(s):
        return min(w_turned_by(s) + min(s + 1, 2), w_chunks)

    def x_due(tile, s, ahead):
        due = []
        for start, c in chunk_starts.items():
            if s == (start + 1 if c == 0 else start):
                if c + ahead < chunks:
                    due.append((tile, c + ahead))
                elif not tile.last:
                    due.append((tile.next(), c + ahead - chunks))
        return due

    def transposes_due(tile, s):
        due = []
        if tile.first:
            if s == 0:
                due.append(("x", tile, 0))
            due += [("w", k) for k in range(w_turned_by(s - 1), w_turned_by(s))]
        return due + [("x", of, c) for of, c in x_due(tile, s, 1)]

    def splits_due(tile, s):
        due = []
        if tile.first:
            if s == 0:
                due.append(("x", tile, 0))
            due += [("w", k) for k in range(w_split_by(s - 1), w_split_by(s))]
            if s == 0:
                due.append(("x", tile, 1))
        return due + [("x", of, c) for of, c in x_due(tile, s, 2)]

    def each_tile(eng, emit):
        emit(Tile(0, 0, 0))
        with eng.Fori(0, (tiles - 2) // 2) as t:
            emit(Tile(2 * t + 1, 1, t))
            emit(Tile(2 * t + 2, 0, t + 1))
        emit(Tile(tiles - 1, 1, tiles // 2 - 1, last=True))

    with ExitStack() as ctx:
        def sb(name, shape, dt=F32):
            return ctx.enter_context(nc.sbuf_tensor(name, shape, dt))

        def psum(name, cols):
            return ctx.enter_context(nc.psum_tensor(name, [P, cols], F32))

        def sem(name):
            return ctx.enter_context(nc.semaphore(name))

        w_t = sb("w_t", [P, pairs * dim], F32R)
        x_sb = [sb(f"x_sb{h}", [P, fields * dim]) for h in range(2)]
        x_parts = [sb(f"x_parts{h}", [P, CHUNK, 3, dim]) for h in range(2)]
        x_t = [sb(f"x_t{h}", [P, CHUNK, 2, P], F32R) for h in range(2)]
        w_parts = [sb(f"w_parts{h}", [P, W_CHUNK // 2, 2, dim]) for h in range(2)]
        ident_sb = sb("ident_sb", [P, P])
        staged = [sb(f"staged{s}", [P, slot_pairs * dim]) for s in range(SLOTS)]
        w_in_x = fields * dim // w_cols
        w_extra = sb("w_extra", [P, (W_RING - w_in_x) * w_cols])
        w_early = [staged[slot][:, n * w_cols:(n + 1) * w_cols]
                   for slot in W_SPLIT_SLOTS for n in range(w_per_slot)]
        w_ring = [x_sb[1][:, n * w_cols:(n + 1) * w_cols] for n in range(w_in_x)]
        w_ring += [w_extra[:, n * w_cols:(n + 1) * w_cols] for n in range(W_RING - w_in_x)]

        def w_in(k):
            return w_early[k] if k < len(w_early) else w_ring[(k - len(w_early)) % W_RING]
        proj = [psum(f"proj{b}", 2 * BANK) for b in range(PROJ_BUFS)]
        turned = [psum(f"turned{k}", BANK) for k in range(2)]

        ident_loaded = sem("ident_loaded")
        x_first_loaded = sem("x_first_loaded")
        x_loaded = [sem(f"x_loaded{h}") for h in range(2)]
        w_early_loaded = [sem(f"w_early_loaded{k}") for k in range(len(w_early))]
        w_ring_loaded = [sem(f"w_ring_loaded{r}") for r in range(W_RING)]
        x_hi_done = sem("x_hi_done")
        x_parts_done = sem("x_parts_done")
        x_turned = [sem(f"x_turned{k}") for k in range(2)]
        x_t_done = [sem(f"x_t_done{k}") for k in range(2)]
        w_hi_done = sem("w_hi_done")
        w_lo_done = sem("w_lo_done")
        w_turned = [sem(f"w_turned{k}") for k in range(2)]
        w_t_done = [sem(f"w_t_done{k}") for k in range(2)]
        projected = [sem(f"projected{b}") for b in range(PROJ_BUFS)]
        read_out = [sem(f"read_out{b}") for b in range(PROJ_BUFS)]
        pool_scaled = sem("pool_scaled")
        stored = [sem(f"stored{s}") for s in range(SLOTS)]

        block = ctx.enter_context(nc.Block())

        @block.sync
        def _(sp):
            def emit(tile):
                s = -1
                for g, group in enumerate(groups):
                    first, end = group_range(group)
                    s += len(group)
                    by_dve = s
                    if s in pool_steps and not tile.first:
                        sp.wait_ge(pool_scaled, (tile.number - 1) * len(pool_steps) + pool_steps.index(s) + 1)
                        by_dve = s - 1
                    sp.wait_ge(read_out[by_dve % PROJ_BUFS], tile.number * uses + by_dve // PROJ_BUFS + 1)
                    sp.dma_start(out[bass.ds(tile.number * P, P), first * dim:end * dim],
                                 staged[g % SLOTS][:, 0:(end - first) * dim]).then_inc(stored[g % SLOTS], 16)

            def load_x(tile):
                sp.wait_ge(x_parts_done, (tile.number + 1) * 2 * chunks)
                sp.dma_start(x_sb[tile.parity][:], x[bass.ds((tile.number + 2) * P, P), :]
                             ).then_inc(x_loaded[tile.parity], 16)

            first_cols = CHUNK * dim
            sp.dma_start(x_sb[0][:, 0:first_cols], x[0:P, 0:first_cols]).then_inc(x_first_loaded, 16)
            for k in range(len(w_early) + W_RING):
                loaded = w_early_loaded[k] if k < len(w_early) else w_ring_loaded[k - len(w_early)]
                sp.dma_start(w_in(k), w[:, k * w_cols:(k + 1) * w_cols]).then_inc(loaded, 16)
                if k == 0:
                    sp.dma_start(x_sb[0][:, first_cols:], x[0:P, first_cols:]).then_inc(x_loaded[0], 16)
            tile = Tile(0, 0, 0)
            emit(tile)
            load_x(tile)
            with sp.Fori(0, (tiles - 4) // 2) as t:
                for tile in (Tile(2 * t + 1, 1, t), Tile(2 * t + 2, 0, t + 1)):
                    emit(tile)
                    load_x(tile)
            tile = Tile(tiles - 3, 1, tiles // 2 - 2)
            emit(tile)
            load_x(tile)
            emit(Tile(tiles - 2, 0, tiles // 2 - 1))
            emit(Tile(tiles - 1, 1, tiles // 2 - 1, last=True))
            for slot in range(SLOTS):
                sp.wait_ge(stored[slot], 16 * slot_uses * tiles)

        @block.gpsimd
        def _(pool):
            def split_x(tile, c):
                parts = x_parts[c % 2]
                cols = slice(c * CHUNK * dim, (c + 1) * CHUNK * dim)
                pool.wait_ge(x_hi_done, tile.number * chunks + c + 1)
                nc.gpsimd.tensor_tensor(parts[:, :, 1, :], x_sb[tile.parity][:, cols].rearrange(
                    "p (f d) -> p f d", d=dim), parts[:, :, 0, :], ALU.subtract).then_inc(x_parts_done, 1)
                nc.gpsimd.tensor_copy(parts[:, :, 2, :], parts[:, :, 0, :]).then_inc(x_parts_done, 1)

            def split_w(k):
                pool.wait_ge(w_hi_done, k + 1)
                parts = w_parts[k % 2]
                nc.gpsimd.tensor_tensor(parts[:, :, 1, :], w_in(k).rearrange("p (q d) -> p q d", d=dim),
                                        parts[:, :, 0, :], ALU.subtract).then_inc(w_lo_done, 1)

            def emit(tile):
                for s in range(n_steps):
                    for what in splits_due(tile, s):
                        (split_x if what[0] == "x" else split_w)(*what[1:])
                    if s in pool_steps and not tile.first:
                        i, j0, n = steps[s][0]
                        g = s // 2
                        to = (pair_index(i, j0, fields) - group_range(groups[g])[0]) * dim
                        product = staged[g % SLOTS][:, to:to + n * dim]
                        pool.wait_ge(read_out[s % PROJ_BUFS], tile.number * uses + s // PROJ_BUFS + 1)
                        nc.gpsimd.tensor_tensor(product, product,
                                                x_sb[tile.parity][:, j0 * dim:(j0 + n) * dim],
                                                ALU.mult).then_inc(pool_scaled, 1)

            each_tile(pool, emit)

        @block.scalar
        def _(act):
            act.dma_start(ident_sb[:], ident).then_inc(ident_loaded, 16)

            def emit(tile):
                for s in range(n_steps):
                    for what in transposes_due(tile, s):
                        for k in range(2):
                            if what[0] == "x":
                                _, of, c = what
                                act.wait_ge(x_turned[k], of.number * chunks + c + 1)
                                nc.scalar.activation(x_t[c % 2][:, 2 * k:2 * k + 2, :, :].rearrange(
                                    "p f v b -> p (f v b)"), turned[k][:], ACT.Copy).then_inc(x_t_done[k], 1)
                            else:
                                chunk = what[1]
                                act.wait_ge(w_turned[k], chunk + 1)
                                at = chunk * W_CHUNK * dim + k * BANK
                                nc.scalar.activation(w_t[:, at:at + BANK], turned[k][:],
                                                     ACT.Copy).then_inc(w_t_done[k], 1)
                        if what[0] == "w" and what[1] >= len(w_early):
                            new = what[1] + W_RING
                            act.wait_ge(w_lo_done, what[1] + 1)
                            if new < w_chunks:
                                act.dma_start(w_in(new), w[:, new * w_cols:(new + 1) * w_cols]
                                              ).then_inc(w_ring_loaded[(what[1] - len(w_early)) % W_RING], 16)
                            if what[1] == w_chunks - 1:
                                act.dma_start(x_sb[1][:], x[P:2 * P, :]).then_inc(x_loaded[1], 16)
                    if s in pool_steps and not tile.first:
                        i, j0, n = steps[s][0]
                        g = s // 2
                        slot, buf = g % SLOTS, s % PROJ_BUFS
                        to = (pair_index(i, j0, fields) - group_range(groups[g])[0]) * dim
                        act.wait_ge(stored[slot], tile.number * 16 * slot_uses + 16 * (g // SLOTS))
                        act.wait_ge(projected[buf], tile.number * uses + s // PROJ_BUFS + 1)
                        nc.scalar.activation(staged[slot][:, to:to + n * dim], proj[buf][:, 0:n * dim],
                                             ACT.Copy).then_inc(read_out[buf], 1)

            each_tile(act, emit)

        @block.tensor
        def _(pe):
            turned_before = [None]

            def transpose(what):
                before = turned_before[0]
                turned_before[0] = what
                if what[0] == "x":
                    _, of, c = what
                    pe.wait_ge(x_parts_done, (of.number * chunks + c + 1) * 2)
                else:
                    pe.wait_ge(w_lo_done, what[1] + 1)
                for k in range(2):
                    if before is not None and before[0] == "w":
                        pe.wait_ge(w_t_done[k], before[1] + 1)
                    elif before is not None:
                        pe.wait_ge(x_t_done[k], before[1].number * chunks + before[2] + 1)
                    for n in range(BANK // P):
                        if what[0] == "x":
                            part = n % 2
                            parts = x_parts[c % 2][:, 2 * k + n // 2, part:part + 2, :]
                        else:
                            parts = w_parts[what[1] % 2][:, k * (BANK // P) + n, :, :]
                        last = nc.tensor.transpose(turned[k][:, n * P:(n + 1) * P],
                                                   parts.rearrange("p v d -> p (v d)"), ident_sb[:])
                    last.then_inc(x_turned[k] if what[0] == "x" else w_turned[k], 1)

            def project(tile, s):
                buf = s % PROJ_BUFS
                if not (tile.first and s < PROJ_BUFS):
                    pe.wait_ge(read_out[buf], tile.number * uses + s // PROJ_BUFS)
                for (i, j0, n), at in zip(steps[s], place(steps[s], dim)):
                    col = pair_index(i, j0, fields) * dim
                    left = n * dim
                    while left:
                        width = min(left, BANK - at % BANK)
                        for part in range(2):
                            last = nc.tensor.matmul(
                                proj[buf][:, at:at + width], x_t[i // CHUNK % 2][:, i % CHUNK, part, :],
                                w_t[:, col:col + width], start=part == 0, stop=part == 1)
                        at, col, left = at + width, col + width, left - width
                last.then_inc(projected[buf], 1)

            def emit(tile):
                if not tile.first:
                    turned_before[0] = ("x", tile, 0)
                for s in range(n_steps):
                    for what in transposes_due(tile, s):
                        transpose(what)
                    if s in chunk_starts:
                        for k in range(2):
                            pe.wait_ge(x_t_done[k], tile.number * chunks + chunk_starts[s] + 1)
                    if tile.first:
                        for k in range(2):
                            pe.wait_ge(w_t_done[k], w_needed[s] + 1)
                    project(tile, s)

            pe.wait_ge(ident_loaded, 16)
            for _ in range(WARM_UP):
                nc.tensor.transpose(turned[0][:, 0:P], ident_sb[:], ident_sb[:])
            each_tile(pe, emit)

        @block.vector
        def _(dve):
            def split_x(tile, c):
                if tile.first and c == 0:
                    dve.wait_ge(x_first_loaded, 16)
                elif c == (1 if tile.first else 0):
                    dve.wait_ge(x_loaded[tile.parity], 16 * tile.half + 16)
                if not (tile.first and c < 2):
                    dve.wait_ge(x_turned[1], tile.number * chunks + c - 1)
                cols = slice(c * CHUNK * dim, (c + 1) * CHUNK * dim)
                nc.vector.tensor_scalar(
                    x_parts[c % 2][:, :, 0, :].bitcast(I32),
                    x_sb[tile.parity][:, cols].rearrange("p (f d) -> p f d", d=dim).bitcast(I32),
                    HI_BITS, None, ALU.bitwise_and).then_inc(x_hi_done, 1)

            def split_w(k):
                if k < len(w_early):
                    dve.wait_ge(w_early_loaded[k], 16)
                else:
                    turn, r = divmod(k - len(w_early), W_RING)
                    dve.wait_ge(w_ring_loaded[r], 16 * turn + 16)
                if k >= 2:
                    dve.wait_ge(w_turned[1], k - 1)
                nc.vector.tensor_scalar(
                    w_parts[k % 2][:, :, 0, :].bitcast(I32),
                    w_in(k).rearrange("p (q d) -> p q d", d=dim).bitcast(I32),
                    HI_BITS, None, ALU.bitwise_and).then_inc(w_hi_done, 1)

            def emit(tile):
                s = 0
                for g, group in enumerate(groups):
                    slot = g % SLOTS
                    start = group_range(group)[0]
                    if not (tile.first and g < SLOTS):
                        dve.wait_ge(stored[slot], tile.number * 16 * slot_uses + 16 * (g // SLOTS))
                    if tile.first and slot in W_SPLIT_SLOTS and g < SLOTS:
                        dve.wait_ge(w_lo_done, (W_SPLIT_SLOTS.index(slot) + 1) * w_per_slot)
                    for step in group:
                        for what in splits_due(tile, s):
                            (split_x if what[0] == "x" else split_w)(*what[1:])
                        if s in pool_steps and not tile.first:
                            s += 1
                            continue
                        buf = s % PROJ_BUFS
                        dve.wait_ge(projected[buf], tile.number * uses + s // PROJ_BUFS + 1)
                        for (i, j0, n), at in zip(step, place(step, dim)):
                            to = (pair_index(i, j0, fields) - start) * dim
                            last = nc.vector.tensor_tensor(
                                staged[slot][:, to:to + n * dim], proj[buf][:, at:at + n * dim],
                                x_sb[tile.parity][:, j0 * dim:(j0 + n) * dim], ALU.mult)
                        last.then_inc(read_out[buf], 1)
                        s += 1

            each_tile(dve, emit)


def kernel(r_x, L0_rec_W):
    import numpy as np
    import concourse.bacc as bacc
    from concourse.bass_utils import run_bass_kernel_spmd

    batch, fields, dim = r_x.shape
    pairs = L0_rec_W.shape[0]
    w = np.ascontiguousarray(np.asarray(L0_rec_W).reshape(pairs // 2, 2 * dim, dim).transpose(1, 0, 2))
    arrays = {
        "x_dram": np.ascontiguousarray(r_x).reshape(batch, fields * dim),
        "w_dram": w.reshape(2 * dim, pairs // 2 * dim),
        "ident_dram": np.eye(P, dtype=np.float32),
    }
    nc = bacc.Bacc("TRN2", target_bir_lowering=False, num_devices=1)
    aps = [nc.dram_tensor(n, a.shape, F32, kind="ExternalInput").ap() for n, a in arrays.items()]
    out = nc.dram_tensor("out_dram", (batch, pairs * dim), F32, kind="ExternalOutput").ap()
    field_pair_project(nc, *aps, out, fields, dim)
    r = run_bass_kernel_spmd(nc, [arrays], core_ids=[0])
    return r.results[0]["out_dram"].reshape(batch, pairs, dim)
```
